# Optimizing a Trainium2 kernel written in Bass

```python
import numpy as np
import jax
import jax.numpy as jnp

def _softmax(x, axis=-1):
    return jax.nn.softmax(x, axis=axis)

def _gelu(x):
    return jax.nn.gelu(x, approximate=True)

def _silu(x):
    return jax.nn.silu(x)

def _sigmoid(x):
    return jax.nn.sigmoid(x)

def _layernorm(x, axis=-1, eps=1e-05):
    m = jnp.mean(x, axis=axis, keepdims=True)
    v = jnp.var(x, axis=axis, keepdims=True)
    return (x - m) / jnp.sqrt(v + eps)

def _scatter_add(tgt, idx, src, axis=0):
    return tgt.at[idx].add(src)

def _segment_sum(src, seg, n):
    return jax.ops.segment_sum(src, seg, n)
kernel_name = 'mk_recurrent_d1_jaxref_r4_a7174d'

def setup_inputs(seed: int=0):
    np.random.seed(seed)
    _w = jnp.asarray

    def _L0_attn_setup():
        import math
        import jax, jax.numpy as jnp
        import numpy as np
        N_HEADS = 16
        N_KV_HEADS = 4
        HEAD_DIM = 128
        D_MODEL = 512
        THETA = 10000.0
        SCALE_BASE = 128

        def _rope_cos_sin(seq_len, head_dim, theta):
            half = head_dim // 2
            inv_freq = 1.0 / theta ** (jnp.arange(half, dtype=jnp.float32) / half)
            pos = jnp.arange(seq_len, dtype=jnp.float32)
            freqs = jnp.outer(pos, inv_freq)
            freqs = jnp.concatenate([freqs, freqs], axis=-1)
            return (jnp.cos(freqs), jnp.sin(freqs))

        def _rotate_half(x):
            half = x.shape[-1] // 2
            return jnp.concatenate([-x[..., half:], x[..., :half]], axis=-1)

        def _xpos_scale(seq_len, head_dim, scale_base):
            pos = jnp.arange(seq_len, dtype=jnp.float32)
            scale = (pos + scale_base / 2.0) / scale_base
            half = head_dim // 2
            s = jnp.broadcast_to(scale[:, None], (seq_len, half))
            return jnp.stack([s, 1.0 / s], axis=-1).reshape(seq_len, head_dim)
        key = jax.random.key(seed)
        ks = jax.random.split(key, 5)
        std = 1.0 / math.sqrt(D_MODEL)
        x = jax.random.normal(ks[0], (2, 512, D_MODEL), dtype=jnp.float32)
        Wq = jax.random.normal(ks[1], (D_MODEL, N_HEADS * HEAD_DIM), dtype=jnp.float32) * std
        Wk = jax.random.normal(ks[2], (D_MODEL, N_KV_HEADS * HEAD_DIM), dtype=jnp.float32) * std
        Wv = jax.random.normal(ks[3], (D_MODEL, N_KV_HEADS * HEAD_DIM), dtype=jnp.float32) * std
        Wo = jax.random.normal(ks[4], (N_HEADS * HEAD_DIM, D_MODEL), dtype=jnp.float32) * std
        return {'x': x, 'Wq': Wq, 'Wk': Wk, 'Wv': Wv, 'Wo': Wo}
    _L0_attn_in = _L0_attn_setup()

    def _L0_ffn_setup():
        import jax, jax.numpy as jnp
        import numpy as np
        E = 8
        TOP_K = 2
        D = 512
        M = 1792
        B, S = (2, 512)
        key = jax.random.key(seed)
        kx, kg, k1, k2, k3 = jax.random.split(key, 5)
        x = jax.random.normal(kx, (B, S, D), dtype=jnp.float32)
        gate_w = jax.random.normal(kg, (D, E), dtype=jnp.float32) / np.sqrt(D)
        w1 = jax.random.normal(k1, (E, D, M), dtype=jnp.float32) / np.sqrt(D)
        w2 = jax.random.normal(k2, (E, M, D), dtype=jnp.float32) / np.sqrt(M)
        w3 = jax.random.normal(k3, (E, D, M), dtype=jnp.float32) / np.sqrt(D)
        return {'x': x, 'gate_w': gate_w, 'w1': w1, 'w2': w2, 'w3': w3}
    _L0_ffn_in = _L0_ffn_setup()
    _d = {'L0_attn_x': _L0_attn_in['x'], 'L0_attn_Wq': _L0_attn_in['Wq'], 'L0_attn_Wk': _L0_attn_in['Wk'], 'L0_attn_Wv': _L0_attn_in['Wv'], 'L0_attn_Wo': _L0_attn_in['Wo'], 'L0_ffn_gate_w': _L0_ffn_in['gate_w'], 'L0_ffn_w1': _L0_ffn_in['w1'], 'L0_ffn_w2': _L0_ffn_in['w2'], 'L0_ffn_w3': _L0_ffn_in['w3']}
    _x0 = _d['L0_attn_x']
    _d['L0_attn_x'] = jax.random.normal(jax.random.fold_in(jax.random.key(seed), 1), (4, 1024, 512), dtype=_x0.dtype)
    del _x0
    return _d

def reference(L0_attn_x, L0_attn_Wq, L0_attn_Wk, L0_attn_Wv, L0_attn_Wo, L0_ffn_gate_w, L0_ffn_w1, L0_ffn_w2, L0_ffn_w3):

    def _L0_attn_ref(x, Wq, Wk, Wv, Wo):
        import math
        import jax, jax.numpy as jnp
        import numpy as np
        N_HEADS = 16
        N_KV_HEADS = 4
        HEAD_DIM = 128
        D_MODEL = 512
        THETA = 10000.0
        SCALE_BASE = 128

        def _rope_cos_sin(seq_len, head_dim, theta):
            half = head_dim // 2
            inv_freq = 1.0 / theta ** (jnp.arange(half, dtype=jnp.float32) / half)
            pos = jnp.arange(seq_len, dtype=jnp.float32)
            freqs = jnp.outer(pos, inv_freq)
            freqs = jnp.concatenate([freqs, freqs], axis=-1)
            return (jnp.cos(freqs), jnp.sin(freqs))

        def _rotate_half(x):
            half = x.shape[-1] // 2
            return jnp.concatenate([-x[..., half:], x[..., :half]], axis=-1)

        def _xpos_scale(seq_len, head_dim, scale_base):
            pos = jnp.arange(seq_len, dtype=jnp.float32)
            scale = (pos + scale_base / 2.0) / scale_base
            half = head_dim // 2
            s = jnp.broadcast_to(scale[:, None], (seq_len, half))
            return jnp.stack([s, 1.0 / s], axis=-1).reshape(seq_len, head_dim)
        B, S, _ = x.shape
        kv_groups = N_HEADS // N_KV_HEADS
        q = (x @ Wq).reshape(B, S, N_HEADS, HEAD_DIM).transpose(0, 2, 1, 3)
        k = (x @ Wk).reshape(B, S, N_KV_HEADS, HEAD_DIM).transpose(0, 2, 1, 3)
        v = (x @ Wv).reshape(B, S, N_KV_HEADS, HEAD_DIM).transpose(0, 2, 1, 3)
        cos, sin = _rope_cos_sin(S, HEAD_DIM, THETA)
        cos = cos[None, None]
        sin = sin[None, None]
        q = q * cos + _rotate_half(q) * sin
        k = k * cos + _rotate_half(k) * sin
        xscale = _xpos_scale(S, HEAD_DIM, SCALE_BASE)[None, None]
        q = q * xscale
        k = k * (1.0 / xscale)
        k = jnp.repeat(k, kv_groups, axis=1)
        v = jnp.repeat(v, kv_groups, axis=1)
        scale = math.sqrt(HEAD_DIM)
        scores = jnp.einsum('bhqd,bhkd->bhqk', q, k) / scale
        causal = jnp.tril(jnp.ones((S, S), dtype=bool))
        scores = jnp.where(causal[None, None], scores, -jnp.inf)
        attn = jax.nn.softmax(scores, axis=-1)
        out = jnp.einsum('bhqk,bhkd->bhqd', attn, v)
        out = out.transpose(0, 2, 1, 3).reshape(B, S, N_HEADS * HEAD_DIM)
        return out @ Wo

    def _L0_ffn_ref(x, gate_w, w1, w2, w3):
        import jax, jax.numpy as jnp
        import numpy as np
        E = 8
        TOP_K = 2
        D = 512
        M = 1792
        B, S = (2, 512)
        b, s, d = x.shape
        x_flat = x.reshape(-1, d)
        router_logits = x_flat @ gate_w
        router_probs = jax.nn.softmax(router_logits, axis=-1)
        topk_w, topk_idx = jax.lax.top_k(router_probs, TOP_K)
        topk_w = topk_w / jnp.sum(topk_w, axis=-1, keepdims=True)
        idx_flat = topk_idx.reshape(-1)
        sort_idx = jnp.argsort(idx_flat)
        x_rep_sort = jnp.take(x_flat, sort_idx // TOP_K, axis=0)
        group_sizes = jnp.bincount(idx_flat, length=E).astype(jnp.int32)
        h = jax.lax.ragged_dot(x_rep_sort, w1, group_sizes)
        h = jax.nn.silu(h) * jax.lax.ragged_dot(x_rep_sort, w3, group_sizes)
        out_sort = jax.lax.ragged_dot(h, w2, group_sizes)
        inv_sort_idx = jnp.argsort(sort_idx)
        out_rep = jnp.take(out_sort, inv_sort_idx, axis=0).reshape(-1, TOP_K, d)
        out = jnp.einsum('tkd,tk->td', out_rep, topk_w)
        return out.reshape(b, s, d)
    x = L0_attn_x
    xn = _layernorm(x, axis=-1)
    s = _L0_attn_ref(xn, L0_attn_Wq, L0_attn_Wk, L0_attn_Wv, L0_attn_Wo)
    g = _silu(_L0_ffn_ref(xn, L0_ffn_gate_w, L0_ffn_w1, L0_ffn_w2, L0_ffn_w3))
    x = x + s * g
    return x

_drawn_inputs = setup_inputs


def setup_inputs(seed=0):
    import zlib

    import numpy as np

    out = dict(_drawn_inputs(seed))
    spreads = {}
    factors = {}
    for name, (base, spread) in spreads.items():
        noise = np.random.default_rng([zlib.crc32(name.encode()), seed]).standard_normal(out[name].shape)
        drawn = base * np.exp(spread * noise) if base else spread * noise
        out[name] = jnp.asarray(drawn.astype(out[name].dtype))
    for name, factor in factors.items():
        out[name] = (out[name] * factor).astype(out[name].dtype)
    return out
```

```python
from contextlib import ExitStack

import numpy as np

import concourse.bass as bass
from concourse import mybir

F32 = mybir.dt.float32
F32R = mybir.dt.float32r
I32 = mybir.dt.int32
ALU = mybir.AluOpType
ACT = mybir.ActivationFunctionType
AX_X = mybir.AxisListType.X

P = 128
BATCH, SEQ, DM = 4, 1024, 512
TOKENS = BATCH * SEQ
TILES = TOKENS // P
SEQ_TILES = SEQ // P
DC = DM // P
HEADS, KV_HEADS, HD = 16, 4, 128
GROUP = HEADS // KV_HEADS
EXPERTS, MLP = 8, 1792
HALVES = 2
HM = MLP // HALVES
MC = HM // P
HN = HM // 2
MIN_BLOCKS = 3
FULL_BLOCKS = 2 * TOKENS // P
BLOCKS = FULL_BLOCKS + MIN_BLOCKS * EXPERTS
SLOTS = BLOCKS * P
PAD_ROW = TOKENS
EPS = 1e-5
NEG = -1.0e30


class Scratch:

    def __init__(self, nc):
        self.xn = nc.dram_tensor("xn_rows", [TOKENS + P, DM], F32, kind="Internal").ap()
        self.xt_hi = nc.dram_tensor("xt_hi", [DM, TOKENS], F32, kind="Internal").ap()
        self.xt_lo = nc.dram_tensor("xt_lo", [DM, TOKENS], F32, kind="Internal").ap()
        self.slot_token = nc.dram_tensor("slot_token", [SLOTS, 1], I32, kind="Internal").ap()
        self.bounds = nc.dram_tensor("block_bounds", [1, EXPERTS + 1], I32, kind="Internal").ap()
        self.pos = nc.dram_tensor("slot_of_token", [P, 2 * TILES], I32, kind="Internal").ap()
        self.weight = nc.dram_tensor("weight_of_token", [P, 2 * TILES], F32, kind="Internal").ap()
        self.y = [nc.dram_tensor(f"expert_out{h}", [SLOTS + P, DM], F32, kind="Internal").ap()
                  for h in range(HALVES)]


def make_identity(pool, ident, done):
    pool.memset(ident[:, :], 0.0).then_inc(done, 1)
    pool.wait_ge(done, 1)
    pool.affine_select(out=ident[:, :], in_=ident[:, :], compare_op=ALU.not_equal, fill=1.0,
                       base=0, pattern=[[-1, P]], channel_multiplier=1).then_inc(done, 1)


def close_wait(eng, passed):
    eng.sem_inc(passed, 1)


def stage_route(nc, x, gate_w, sc):
    GT = 4
    STEPS = TILES // GT
    TE = TILES * EXPERTS
    x_rows = x.rearrange("b s d -> (b s) d")
    with ExitStack() as ctx:
        def sb(name, shape, dt=F32):
            return ctx.enter_context(nc.sbuf_tensor(name, shape, dt))

        def sem(name):
            return ctx.enter_context(nc.semaphore(name))

        ident = sb("r_ident", [P, P])
        before = sb("r_before", [P, P])
        ones = sb("r_ones", [P, P])
        zrow = sb("r_zrow", [P, DM])
        xin = sb("r_xin", [P, 2 * GT, DM])
        xn = sb("r_xn", [P, GT, DM])
        stats = sb("r_stats", [P, GT, 6])
        mv = sb("r_mv", [P, GT, 2])
        sd = sb("r_sd", [P, GT])
        ve = sb("r_ve", [P, GT])
        r0 = sb("r_r0", [P, GT])
        r1 = sb("r_r1", [P, GT])
        xth = sb("r_xth", [P, DC, GT * P], F32R)
        xtl = sb("r_xtl", [P, DC, GT * P], F32R)
        gw = sb("r_gw", [P, DC, EXPERTS])
        gwh = sb("r_gwh", [P, DC, EXPERTS], F32R)
        gwl = sb("r_gwl", [P, DC, EXPERTS], F32R)
        lg = sb("r_logits", [P, TE])
        iota_i = sb("r_iota_i", [P, TE], I32)
        iota_e = sb("r_iota_e", [P, TE])
        tok = sb("r_tok", [P, TILES], I32)
        first = sb("r_first", [P, EXPERTS * TILES])
        t1 = sb("r_t1", [P, TE])
        t2 = sb("r_t2", [P, TE])
        one1 = sb("r_one1", [P, TE])
        one2 = sb("r_one2", [P, TE])
        both = sb("r_both", [P, TE])
        m1 = sb("r_m1", [P, TILES])
        m2 = sb("r_m2", [P, TILES])
        i1 = sb("r_i1", [P, TILES])
        i2 = sb("r_i2", [P, TILES])
        wt = sb("r_wt", [P, 2, TILES])
        tot = sb("r_tot", [P, TE])
        inc = sb("r_inc", [P, TE])
        nb_i = sb("r_nb_i", [P, EXPERTS], I32)
        nb_j = sb("r_nb_j", [P, EXPERTS], I32)
        nb = sb("r_nb", [P, EXPERTS])
        ends = sb("r_ends", [P, EXPERTS])
        base = sb("r_base", [P, EXPERTS])
        bnd = sb("r_bnd", [P, EXPERTS + 1], I32)
        posf = sb("r_posf", [P, 2, TILES])
        posi = sb("r_posi", [P, 2, TILES], I32)
        idx = sb("r_idx", [P, GT, 2], I32)
        src = sb("r_src", [P, GT], I32)
        pad = sb("r_pad", [BLOCKS, P], I32)

        ptx = [ctx.enter_context(nc.psum_tensor(f"r_ptx{c}", [P, 512], F32)) for c in range(DC)]
        plg = ctx.enter_context(nc.psum_tensor("r_plg", [P, 512], F32))
        pcnt = ctx.enter_context(nc.psum_tensor("r_pcnt", [P, 512], F32))
        ptot = ctx.enter_context(nc.psum_tensor("r_ptot", [P, 512], F32))

        ident_done, before_done, const_done = sem("r_ident_done"), sem("r_before_done"), sem("r_const_done")
        gate_loaded, x_loaded = sem("r_gate_loaded"), sem("r_x_loaded")
        gate_hi, gate_split = sem("r_gate_hi"), sem("r_gate_split")
        xn_ready, xn_stored = sem("r_xn_ready"), sem("r_xn_stored")
        stat, sqrt_in, sqrt_out = sem("r_stat"), sem("r_sqrt_in"), sem("r_sqrt_out")
        turned, hi_ready, lo_ready = sem("r_turned"), sem("r_hi_ready"), sem("r_lo_ready")
        hi_stored, lo_stored = sem("r_hi_stored"), sem("r_lo_stored")
        logits_ready, logits_kept = sem("r_logits_ready"), sem("r_logits_kept")
        zero_ready, zero_stored = sem("r_zero_ready"), sem("r_zero_stored")
        pad_ready, pad_stored = sem("r_pad_ready"), sem("r_pad_stored")
        passed = sem("r_passed")
        chain = sem("r_chain")
        both_ready, counted = sem("r_both_ready"), sem("r_counted")
        gap_ready, exp_ready = sem("r_gap_ready"), sem("r_exp_ready")
        tables_ready, tables_stored = sem("r_tables_ready"), sem("r_tables_stored")
        idx_ready, scattered = sem("r_idx_ready"), sem("r_scattered")

        block = ctx.enter_context(nc.Block())

        @block.sync
        def _(sp):
            def load(g):
                nc.sync.dma_start(xin[:, bass.ds((g % 2) * GT, GT), :],
                                  x_rows[bass.ds(g * (GT * P), GT * P), :].rearrange("(c p) d -> p c d", p=P)
                                  ).then_inc(x_loaded, 16)

            def store(g):
                sp.wait_ge(xn_ready, g + 1)
                nc.sync.dma_start(sc.xn[bass.ds(g * (GT * P), GT * P), :].rearrange("(c p) d -> p c d", p=P),
                                  xn[:, :, :]).then_inc(xn_stored, 16)

            def store_turned(g):
                sp.wait_ge(hi_ready, DC * (g + 1))
                close_wait(sp, passed)
                nc.sync.dma_start(sc.xt_hi[:, bass.ds(g * (GT * P), GT * P)].rearrange("(c p) t -> p c t", p=P),
                                  xth[:, :, :].bitcast(F32)).then_inc(hi_stored, 16)
                sp.wait_ge(lo_ready, DC * (g + 1))
                nc.sync.dma_start(sc.xt_lo[:, bass.ds(g * (GT * P), GT * P)].rearrange("(c p) t -> p c t", p=P),
                                  xtl[:, :, :].bitcast(F32)).then_inc(lo_stored, 16)

            nc.sync.dma_start(gw[:, :, :], gate_w.rearrange("(c p) e -> p c e", p=P)).then_inc(gate_loaded, 16)
            load(0)
            sp.wait_ge(x_loaded, 16)
            load(1)
            sp.wait_ge(zero_ready, 1)
            nc.sync.dma_start(sc.xn[TOKENS:TOKENS + P, :], zrow[:, :]).then_inc(zero_stored, 16)
            with sp.Fori(0, STEPS - 2) as g:
                store(g)
                sp.wait_ge(x_loaded, 16 * (g + 2))
                close_wait(sp, passed)
                load(g + 2)
                store_turned(g)
            for g in (STEPS - 2, STEPS - 1):
                store(g)
                store_turned(g)
            sp.wait_ge(pad_ready, 1)
            nc.sync.dma_start(sc.slot_token.rearrange("(b p) o -> b (p o)", p=P), pad[:, :]).then_inc(pad_stored, 16)
            nc.sync.dma_start(sc.y[0][0:P, :], zrow[:, :]).then_inc(zero_stored, 16)
            for y in sc.y:
                nc.sync.dma_start(y[P * (FULL_BLOCKS + 1):, :].rearrange("(c p) d -> p c d", p=P),
                                  zrow[:, :].unsqueeze(1).to_broadcast([P, BLOCKS - FULL_BLOCKS, DM])
                                  ).then_inc(zero_stored, 16)
            sp.wait_ge(tables_ready, 1)
            nc.sync.dma_start(sc.bounds, bnd[0:1, :]).then_inc(tables_stored, 16)
            nc.sync.dma_start(sc.pos, posi[:, :, :].rearrange("p k t -> p (k t)")).then_inc(tables_stored, 16)
            nc.sync.dma_start(sc.weight, wt[:, :, :].rearrange("p k t -> p (k t)")).then_inc(tables_stored, 16)
            sp.wait_ge(tables_stored, 48)
            sp.wait_ge(zero_stored, 64)
            sp.wait_ge(pad_stored, 16)
            sp.wait_ge(xn_stored, 16 * STEPS)
            sp.wait_ge(hi_stored, 16 * STEPS)
            sp.wait_ge(lo_stored, 16 * STEPS)

        @block.gpsimd
        def _(pool):
            make_identity(pool, ident, ident_done)
            nc.gpsimd.memset(ones[:, :], 1.0).then_inc(const_done, 1)
            pool.wait_ge(const_done, 1)
            nc.gpsimd.affine_select(out=before[:, :], in_=ones[:, :], compare_op=ALU.is_gt, fill=0.0, base=0,
                                    pattern=[[1, P]], channel_multiplier=-1).then_inc(before_done, 1)
            nc.gpsimd.memset(zrow[:, :], 0.0).then_inc(zero_ready, 1)
            nc.gpsimd.memset(pad[:, :], PAD_ROW).then_inc(pad_ready, 1)
            nc.gpsimd.iota(iota_i[:, :], pattern=[[0, TILES], [1, EXPERTS]], base=-EXPERTS,
                           channel_multiplier=0).then_inc(const_done, 1)
            nc.gpsimd.iota(tok[:, :], pattern=[[P, TILES]], base=0, channel_multiplier=1).then_inc(const_done, 1)
            pool.wait_ge(const_done, 3)
            nc.gpsimd.tensor_copy(iota_e[:, :], iota_i[:, :]).then_inc(const_done, 1)
            nc.gpsimd.memset(first[:, :], 1.0).then_inc(const_done, 1)
            pool.wait_ge(const_done, 5)
            nc.gpsimd.memset(first[:, 0:EXPERTS * TILES:TILES], 0.0).then_inc(const_done, 1)

            pool.wait_ge(pad_stored, 16)
            pool.wait_ge(tables_ready, 1)
            with pool.Fori(0, STEPS) as g:
                pool.wait_ge(scattered, 16 * 2 * GT * g)
                for k in range(2):
                    nc.gpsimd.tensor_copy(idx[:, :, k], posi[:, k, bass.ds(g * GT, GT)]).then_inc(idx_ready, 1)
                nc.gpsimd.tensor_copy(src[:, :], tok[:, bass.ds(g * GT, GT)]).then_inc(idx_ready, 1)
                pool.wait_ge(idx_ready, 3 * (g + 1))
                close_wait(pool, passed)
                for c in range(GT):
                    for k in range(2):
                        nc.gpsimd.indirect_dma_start(
                            sc.slot_token, bass.IndirectOffsetOnAxis(idx[:, c, k:k + 1], 0),
                            src[:, c:c + 1], None).then_inc(scattered, 16)
            pool.wait_ge(scattered, 16 * 2 * TILES)

        @block.scalar
        def _(act):
            act.wait_ge(gate_loaded, 16)
            nc.scalar.activation(gwh[:, :, :], gw[:, :, :], ACT.Copy).then_inc(gate_hi, 1)

            def deviations_and_hi(g):
                act.wait_ge(sqrt_in, g + 1)
                nc.scalar.activation(sd[:, :], ve[:, :], ACT.Sqrt).then_inc(sqrt_out, 1)
                act.wait_ge(logits_ready, g)
                act.wait_ge(hi_stored, 16 * g)
                for c in range(DC):
                    act.wait_ge(turned, DC * g + c + 1)
                    nc.scalar.activation(xth[:, c, :], ptx[c][:, :], ACT.Copy).then_inc(hi_ready, 1)

            def keep_logits(g):
                act.wait_ge(logits_ready, g + 1)
                nc.scalar.activation(lg[:, bass.ds(g * (GT * EXPERTS), GT * EXPERTS)], plg[:, 0:GT * EXPERTS],
                                     ACT.Copy).then_inc(logits_kept, 1)

            deviations_and_hi(0)
            with act.Fori(1, STEPS) as g:
                deviations_and_hi(g)
                keep_logits(g - 1)
            keep_logits(STEPS - 1)
            act.wait_ge(gap_ready, 1)
            nc.scalar.activation(m2[:, :], m1[:, :], ACT.Exp).then_inc(exp_ready, 1)

        @block.tensor
        def _(pe):
            pe.wait_ge(ident_done, 2)
            pe.wait_ge(gate_split, 1)
            with pe.Fori(0, STEPS) as g:
                pe.wait_ge(xn_ready, g + 1)
                for c in range(DC):
                    pe.wait_ge(lo_ready, DC * g)
                    for t in range(GT):
                        last = nc.tensor.transpose(ptx[c][:, t * P:(t + 1) * P], xn[:, t, c * P:(c + 1) * P],
                                                   ident[:, :])
                    last.then_inc(turned, 1)
                pe.wait_ge(hi_ready, DC * (g + 1))
                pe.wait_ge(lo_ready, DC * (g + 1))
                pe.wait_ge(logits_kept, g)
                for t in range(GT):
                    n = 0
                    for c in range(DC):
                        for xs in (xth, xtl):
                            for ws in (gwh, gwl):
                                last = nc.tensor.matmul(plg[:, t * EXPERTS:(t + 1) * EXPERTS],
                                                        xs[:, c, t * P:(t + 1) * P], ws[:, c, :],
                                                        start=(n == 0), stop=(n == 4 * DC - 1))
                                n += 1
                last.then_inc(logits_ready, 1)
            pe.wait_ge(both_ready, 1)
            pe.wait_ge(before_done, 1)
            nc.tensor.matmul(pcnt[:, 0:TE], before[:, :], both[:, :], start=True, stop=True)
            nc.tensor.matmul(ptot[:, 0:TE], ones[:, :], both[:, :], start=True, stop=True).then_inc(counted, 1)

        @block.vector
        def _(dve):
            dve.wait_ge(gate_hi, 1)
            nc.vector.tensor_tensor(gwl[:, :, :], gw[:, :, :], gwh[:, :, :].bitcast(F32),
                                    ALU.subtract).then_inc(gate_split, 1)
            SN = 7

            def normalise(g):
                def step(ins, n):
                    ins.then_inc(stat, 1)
                    dve.wait_ge(stat, SN * g + n)

                dve.wait_ge(x_loaded, 16 * (g + 1))
                for t in range(GT):
                    last = nc.vector.bn_stats(stats[:, t, :], xin[:, bass.ds((g % 2) * GT + t, 1), :].rearrange("p o d -> p (o d)"))
                step(last, 1)
                close_wait(dve, passed)
                for t in range(GT):
                    last = nc.vector.bn_aggr(mv[:, t, :], stats[:, t, :])
                step(last, 2)
                nc.vector.tensor_scalar(ve[:, :], mv[:, :, 1], EPS, None, ALU.add).then_inc(sqrt_in, 1)
                dve.wait_ge(sqrt_out, g + 1)
                step(nc.vector.reciprocal(r0[:, :], sd[:, :]), 3)
                step(nc.vector.tensor_tensor(r1[:, :], r0[:, :], r0[:, :], ALU.mult), 4)
                step(nc.vector.tensor_tensor(r1[:, :], r1[:, :], ve[:, :], ALU.mult), 5)
                step(nc.vector.tensor_scalar(r1[:, :], r1[:, :], -0.5, 1.5, ALU.mult, ALU.add), 6)
                step(nc.vector.tensor_tensor(r1[:, :], r1[:, :], r0[:, :], ALU.mult), 7)
                dve.wait_ge(turned, DC * g)
                dve.wait_ge(xn_stored, 16 * g)
                for t in range(GT):
                    last = nc.vector.tensor_scalar(xn[:, t, :], xin[:, bass.ds((g % 2) * GT + t, 1), :].rearrange("p o d -> p (o d)"),
                                                   mv[:, t, 0:1], r1[:, t:t + 1], ALU.subtract, ALU.mult)
                last.then_inc(xn_ready, 1)

            def keep_lo(g):
                dve.wait_ge(lo_stored, 16 * g)
                dve.wait_ge(logits_ready, g)
                for c in range(DC):
                    dve.wait_ge(hi_ready, DC * g + c + 1)
                    nc.vector.tensor_tensor(xtl[:, c, :], ptx[c][:, :], xth[:, c, :].bitcast(F32),
                                            ALU.subtract).then_inc(lo_ready, 1)

            normalise(0)
            with dve.Fori(1, STEPS) as g:
                normalise(g)
                keep_lo(g - 1)
            keep_lo(STEPS - 1)

            done = [0]

            def link(ins):
                done[0] += 1
                ins.then_inc(chain, 1)
                dve.wait_ge(chain, done[0])

            def te(a):
                return a[:, :].rearrange("p (t e) -> p t e", e=EXPERTS)

            def et(a):
                return a[:, :].rearrange("p (e t) -> p t e", t=TILES)

            def wide(a):
                return a.unsqueeze(2).to_broadcast([P, TILES, EXPERTS])

            dve.wait_ge(logits_kept, STEPS)
            dve.wait_ge(const_done, 6)
            link(nc.vector.tensor_reduce(m1[:, :], te(lg), AX_X, ALU.max))
            link(nc.vector.tensor_tensor(te(t1), te(lg), wide(m1[:, :]), ALU.is_ge))
            link(nc.vector.tensor_tensor(t1[:, :], t1[:, :], iota_e[:, :], ALU.mult))
            link(nc.vector.tensor_reduce(i1[:, :], te(t1), AX_X, ALU.min))
            link(nc.vector.tensor_tensor(te(one1), te(iota_e), wide(i1[:, :]), ALU.is_equal))
            link(nc.vector.scalar_tensor_tensor(out=t2[:, :], in0=one1[:, :], scalar=NEG, in1=lg[:, :],
                                                op0=ALU.mult, op1=ALU.add))
            link(nc.vector.tensor_reduce(m2[:, :], te(t2), AX_X, ALU.max))
            link(nc.vector.tensor_tensor(te(t1), te(t2), wide(m2[:, :]), ALU.is_ge))
            link(nc.vector.tensor_tensor(t1[:, :], t1[:, :], iota_e[:, :], ALU.mult))
            link(nc.vector.tensor_reduce(i2[:, :], te(t1), AX_X, ALU.min))
            link(nc.vector.tensor_tensor(te(one2), te(iota_e), wide(i2[:, :]), ALU.is_equal))
            nc.vector.tensor_tensor(both[:, :], one1[:, :], one2[:, :], ALU.add).then_inc(both_ready, 1)
            nc.vector.tensor_tensor(m1[:, :], m2[:, :], m1[:, :], ALU.subtract).then_inc(gap_ready, 1)
            dve.wait_ge(exp_ready, 1)
            link(nc.vector.tensor_scalar(i1[:, :], m2[:, :], 1.0, None, ALU.add))
            link(nc.vector.reciprocal(wt[:, 0, :], i1[:, :]))
            link(nc.vector.tensor_tensor(wt[:, 1, :], wt[:, 0, :], m2[:, :], ALU.mult))
            dve.wait_ge(counted, 1)
            link(nc.vector.tensor_copy(et(tot), te(ptot[:, 0:TE])))
            link(nc.vector.tensor_tensor_scan(inc[:, :], first[:, :], tot[:, :], 0.0, ALU.mult, ALU.add))
            link(nc.vector.tensor_scalar(nb_i[:, :], inc[:, TILES - 1:EXPERTS * TILES:TILES], float(P - 1), None,
                                         ALU.add))
            link(nc.vector.tensor_scalar(nb_j[:, :], nb_i[:, :], P.bit_length() - 1, None, ALU.logical_shift_right))
            link(nc.vector.tensor_scalar(nb[:, :], nb_j[:, :], float(MIN_BLOCKS), None, ALU.max))
            link(nc.vector.tensor_tensor_scan(ends[:, :], ones[:, 0:EXPERTS], nb[:, :], 0.0, ALU.mult, ALU.add))
            link(nc.vector.tensor_tensor(base[:, :], ends[:, :], nb[:, :], ALU.subtract))
            link(nc.vector.tensor_copy(bnd[:, 1:EXPERTS + 1], ends[:, :]))
            link(nc.vector.memset(bnd[:, 0:1], 0))
            link(nc.vector.tensor_scalar(base[:, :], base[:, :], float(P), None, ALU.mult))
            link(nc.vector.tensor_tensor(inc[:, :], inc[:, :], tot[:, :], ALU.subtract))
            link(nc.vector.tensor_tensor(inc[:, :].rearrange("p (e t) -> p e t", t=TILES),
                                         inc[:, :].rearrange("p (e t) -> p e t", t=TILES),
                                         base[:, :].unsqueeze(2).to_broadcast([P, EXPERTS, TILES]), ALU.add))
            link(nc.vector.tensor_tensor(te(t1), te(pcnt[:, 0:TE]), et(inc), ALU.add))
            for k, one in enumerate((one1, one2)):
                link(nc.vector.tensor_tensor(t2[:, :], one[:, :], t1[:, :], ALU.mult))
                link(nc.vector.tensor_reduce(posf[:, k, :], te(t2), AX_X, ALU.add))
            nc.vector.tensor_copy(posi[:, :, :], posf[:, :, :]).then_inc(tables_ready, 1)


def stage_experts(nc, w1, w2, w3, sc):
    PIECE = HM
    UP_PIECES = 2 * DC
    DOWN_PIECES = DC
    PIECES = UP_PIECES + DOWN_PIECES
    RING = 3
    with ExitStack() as ctx:
        def sb(name, shape, dt=F32):
            return ctx.enter_context(nc.sbuf_tensor(name, shape, dt))

        def sem(name):
            return ctx.enter_context(nc.semaphore(name))

        ident = sb("e_ident", [P, P])
        bounds = sb("e_bounds", [1, EXPERTS + 1], I32)
        slot_rows = sb("e_slot_rows", [BLOCKS, P], I32)
        slot_rows_f = sb("e_slot_rows_f", [BLOCKS, P])
        slots = sb("e_slots", [P, BLOCKS], I32)
        idx = sb("e_idx", [P, 1], I32)
        up_hi = [sb(f"e_up_hi{h}", [P, 2, DC, HM], F32R) for h in range(HALVES)]
        up_lo = [sb(f"e_up_lo{h}", [P, 2, DC, HM], F32R) for h in range(HALVES)]
        down_hi = [sb(f"e_down_hi{h}", [P, MC, DM], F32R) for h in range(HALVES)]
        down_lo = [sb(f"e_down_lo{h}", [P, MC, DM], F32R) for h in range(HALVES)]
        ring = [sb(f"e_ring{i}", [P, PIECE]) for i in range(RING)]
        xg = sb("e_xg", [P, DM])
        xth = sb("e_xth", [P, DC, P], F32R)
        xtl = sb("e_xtl", [P, DC, P], F32R)
        gate = sb("e_gate", [P, HM])
        h = sb("e_h", [P, HM])
        hth = sb("e_hth", [P, MC, P], F32R)
        htl = sb("e_htl", [P, MC, P], F32R)
        yo = sb("e_yo", [P, DM])

        p_up = [[ctx.enter_context(nc.psum_tensor(f"e_up{c}_{w}", [P, 512], F32)) for w in range(2)]
                for c in range(2)]
        p_ht = [ctx.enter_context(nc.psum_tensor(f"e_ht{i}", [P, 512], F32)) for i in range(2)]
        p_x = ctx.enter_context(nc.psum_tensor("e_px", [P, 512], F32))
        p_y = ctx.enter_context(nc.psum_tensor("e_py", [P, 512], F32))
        HT = [(0, 4), (4, MC)]

        ident_done, bounds_loaded = sem("e_ident_done"), sem("e_bounds_loaded")
        rows_loaded, rows_float, rows_turned, slots_ready = (
            sem("e_rows_loaded"), sem("e_rows_float"), sem("e_rows_turned"), sem("e_slots_ready"))
        piece_loaded = [sem(f"e_piece_loaded{i}") for i in range(RING)]
        piece_hi = [sem(f"e_piece_hi{i}") for i in range(RING)]
        piece_lo = sem("e_piece_lo")
        passed = sem("e_passed")
        h_zero, down_zero = sem("e_h_zero"), sem("e_down_zero")
        idx_ready, gathered = sem("e_idx_ready"), sem("e_gathered")
        x_turned, xh_ready, xl_ready = sem("e_x_turned"), sem("e_xh_ready"), sem("e_xl_ready")
        up_done, gate_ready, h_ready = sem("e_up_done"), sem("e_gate_ready"), sem("e_h_ready")
        h_turned, hh_ready, hl_ready = sem("e_h_turned"), sem("e_hh_ready"), sem("e_hl_ready")
        y_done, y_kept, y_stored = sem("e_y_done"), sem("e_y_kept"), sem("e_y_stored")

        block = ctx.enter_context(nc.Block())

        def passes(eng, first, second, rest):
            eng.wait_ge(bounds_loaded, 16)
            with eng.Fori(0, EXPERTS) as e:
                lo = eng.value_load(bounds[0:1, bass.ds(e, 1)], min_val=0, max_val=BLOCKS - MIN_BLOCKS)
                hi = eng.value_load(bounds[0:1, bass.ds(e + 1, 1)], min_val=MIN_BLOCKS, max_val=BLOCKS)
                for half, shift in ((0, lo), (1, hi)):
                    number = 2 * e + half
                    first(lo + shift, lo, half, number, shift)
                    second(lo + 1 + shift, lo + 1, half, number)
                    with eng.Fori(lo + 2, hi) as row:
                        rest(row + shift, row, half, number)

        def piece_source(q, e, half):
            if q < UP_PIECES:
                w, c = (w1, w3)[q // DC], q % DC
                return w[bass.ds(e, 1), c * P:(c + 1) * P, half * HM:(half + 1) * HM].rearrange("o p n -> (o p) n")
            c = q - UP_PIECES
            return w2[bass.ds(e, 1), half * HM:(half + 1) * HM, c * P:(c + 1) * P].rearrange(
                "o (m p) n -> (o p) m n", p=P)

        def piece_place(up, down, q, half):
            if q < UP_PIECES:
                return up[half][:, q // DC, q % DC, :]
            c = q - UP_PIECES
            return down[half][:, :, c * P:(c + 1) * P]

        def shaped(a, q):
            return a if q < UP_PIECES else a.rearrange("p (m n) -> p m n", m=MC)

        @block.sync
        def _(sp):
            nc.sync.dma_start(bounds[:, :], sc.bounds).then_inc(bounds_loaded, 16)
            nc.sync.dma_start(slot_rows[:, :], sc.slot_token.rearrange("(b p) o -> b (p o)", p=P)
                              ).then_inc(rows_loaded, 16)

            def load(q, e, half, number):
                if number is not None:
                    sp.wait_ge(piece_lo, PIECES * number + q - RING + 1)
                elif q >= RING:
                    sp.wait_ge(piece_lo, q - RING + 1)
                nc.sync.dma_start(shaped(ring[q % RING][:, :], q), piece_source(q, e, half)
                                  ).then_inc(piece_loaded[q % RING], 16)

            for q in range(PIECES):
                load(q, 0, 0, None)
            with sp.Fori(0, EXPERTS) as e:
                nxt = (e + 1) % EXPERTS
                for q in range(PIECES):
                    load(q, e, 1, 2 * e + 1)
                for q in range(PIECES):
                    load(q, nxt, 0, 2 * e + 2)
            sp.wait_ge(piece_lo, PIECES * (2 * EXPERTS + 1))

        def split_hi(act, q, half, number):
            act.wait_ge(piece_loaded[q % RING], 16 * ((PIECES // RING) * number + q // RING + 1))
            nc.scalar.activation(piece_place(up_hi, down_hi, q, half), shaped(ring[q % RING][:, :], q),
                                 ACT.Copy).then_inc(piece_hi[q % RING], 1)

        def split_lo(dve, q, half, number):
            dve.wait_ge(piece_hi[q % RING], (PIECES // RING) * number + q // RING + 1)
            nc.vector.tensor_tensor(piece_place(up_lo, down_lo, q, half), shaped(ring[q % RING][:, :], q),
                                    piece_place(up_hi, down_hi, q, half).bitcast(F32),
                                    ALU.subtract).then_inc(piece_lo, 1)

        @block.gpsimd
        def _(pool):
            make_identity(pool, ident, ident_done)
            nc.gpsimd.memset(down_hi[1][:, :, :].bitcast(F32), 0.0).then_inc(down_zero, 1)
            nc.gpsimd.memset(down_lo[1][:, :, :].bitcast(F32), 0.0).then_inc(down_zero, 1)
            pool.wait_ge(slots_ready, 1)

            def gather(g, row, half, number):
                pool.wait_ge(gathered, 16 * g)
                close_wait(pool, passed)
                nc.gpsimd.tensor_copy(idx[:, :], slots[:, bass.ds(row, 1)]).then_inc(idx_ready, 1)
                pool.wait_ge(x_turned, g)
                pool.wait_ge(idx_ready, g + 1)
                close_wait(pool, passed)
                nc.gpsimd.indirect_dma_start(xg[:, :], None, sc.xn,
                                             bass.IndirectOffsetOnAxis(idx[:, 0:1], 0)).then_inc(gathered, 16)

            passes(pool, lambda g, row, half, number, ended: gather(g, row, half, number), gather, gather)
            total = pool.value_load(bounds[0:1, EXPERTS:EXPERTS + 1], min_val=MIN_BLOCKS * EXPERTS, max_val=BLOCKS)
            gather(2 * total, total - 1, 1, 0)
            pool.wait_ge(gathered, 32 * total + 16)

        @block.tensor
        def _(pe):
            pe.wait_ge(ident_done, 2)
            pe.wait_ge(rows_float, 1)
            nc.tensor.transpose(p_x[:, 0:BLOCKS], slot_rows_f[:, :], ident[0:BLOCKS, 0:BLOCKS]).then_inc(rows_turned, 1)
            pe.wait_ge(slots_ready, 1)

            def turn_x(n):
                pe.wait_ge(gathered, 16 * (n + 1))
                pe.wait_ge(xl_ready, n)
                for c in range(DC):
                    last = nc.tensor.transpose(p_x[:, c * P:(c + 1) * P], xg[:, c * P:(c + 1) * P], ident[:, :])
                last.then_inc(x_turned, 1)

            def up(g, c, buf):
                for w in range(2):
                    n = 0
                    for d in range(DC):
                        for xs, ws in ((xth, up_hi), (xth, up_lo), (xtl, up_hi)):
                            last = nc.tensor.matmul(p_up[c][w][:, 0:HN], xs[:, d, :],
                                                    ws[buf][:, w, d, c * HN:(c + 1) * HN],
                                                    start=(n == 0), stop=(n == 3 * DC - 1))
                            n += 1
                last.then_inc(up_done, 1)

            def turn_h():
                for i, (a, b) in enumerate(HT):
                    for m in range(a, b):
                        last = nc.tensor.transpose(p_ht[i][:, (m - a) * P:(m - a + 1) * P], h[:, m * P:(m + 1) * P],
                                                   ident[:, :])
                    last.then_inc(h_turned, 1)

            def down(buf):
                n = 0
                for m in range(MC):
                    for hs, ws in ((hth, down_hi), (hth, down_lo), (htl, down_hi)):
                        last = nc.tensor.matmul(p_y[:, :], hs[:, m, :], ws[buf][:, m, :],
                                                start=(n == 0), stop=(n == 3 * MC - 1))
                        n += 1
                last.then_inc(y_done, 1)

            def body(g, up_buf, down_buf):
                pe.wait_ge(xl_ready, g + 1)
                pe.wait_ge(h_ready, 2 * g)
                up(g, 0, up_buf)
                turn_h()
                up(g, 1, up_buf)
                turn_x(g + 1)
                pe.wait_ge(hl_ready, 2 * g + 2)
                pe.wait_ge(y_kept, g)
                down(down_buf)

            def first(g, row, half, number, ended):
                pe.wait_ge(piece_lo, PIECES * (number + 1))
                body(g, half, 1 - half)

            def rest(g, row, half, number):
                body(g, half, half)

            pe.wait_ge(h_zero, 1)
            pe.wait_ge(down_zero, 2)
            turn_x(0)
            passes(pe, first, rest, rest)
            total = pe.value_load(bounds[0:1, EXPERTS:EXPERTS + 1], min_val=MIN_BLOCKS * EXPERTS, max_val=BLOCKS)
            pe.wait_ge(h_ready, 4 * total)
            turn_h()
            pe.wait_ge(hl_ready, 4 * total + 2)
            pe.wait_ge(y_kept, 2 * total)
            down(1)

        @block.scalar
        def _(act):
            for q in range(PIECES):
                split_hi(act, q, 0, 0)

            def keep_x(n):
                act.wait_ge(x_turned, n + 1)
                nc.scalar.activation(xth[:, :, :], p_x[:, :].rearrange("p (c t) -> p c t", c=DC),
                                     ACT.Copy).then_inc(xh_ready, 1)

            def keep_h(g):
                act.wait_ge(y_done, g)
                for i, (a, b) in enumerate(HT):
                    act.wait_ge(h_turned, 2 * g + i + 1)
                    nc.scalar.activation(hth[:, a:b, :], p_ht[i][:, 0:(b - a) * P].rearrange("p (m t) -> p m t", t=P),
                                         ACT.Copy).then_inc(hh_ready, 1)

            def keep_y(g, row_end):
                act.wait_ge(y_stored, 16 * g)
                act.wait_ge(y_done, g + 1)
                nc.scalar.activation(yo[:, :], p_y[:, :], ACT.Copy).then_inc(y_kept, 1)

            def body(g, row, half, number, y_half, pieces):
                pieces = list(pieces)

                def some(n):
                    for q in pieces[:n]:
                        split_hi(act, q, 1 - half, number + 1)
                    del pieces[:n]

                act.wait_ge(h_ready, 2 * g)
                act.wait_ge(up_done, 2 * g + 1)
                nc.scalar.activation(gate[:, 0:HN], p_up[0][0][:, 0:HN], ACT.Silu).then_inc(gate_ready, 1)
                keep_h(g)
                some(3)
                act.wait_ge(up_done, 2 * g + 2)
                nc.scalar.activation(gate[:, HN:HM], p_up[1][0][:, 0:HN], ACT.Silu).then_inc(gate_ready, 1)
                keep_x(g + 1)
                some(len(pieces))
                keep_y(g, row)
                act.wait_ge(y_kept, g + 1)
                nc.scalar.dma_start(sc.y[y_half][bass.ds(row * P, P), :], yo[:, :]).then_inc(y_stored, 16)

            keep_x(0)
            passes(act,
                   lambda g, row, half, number, ended: body(g, ended, half, number, 1 - half, range(UP_PIECES)),
                   lambda g, row, half, number: body(g, row, half, number, half, range(UP_PIECES, PIECES)),
                   lambda g, row, half, number: body(g, row, half, number, half, ()))
            total = act.value_load(bounds[0:1, EXPERTS:EXPERTS + 1], min_val=MIN_BLOCKS * EXPERTS, max_val=BLOCKS)
            keep_h(2 * total)
            keep_y(2 * total, total)
            act.wait_ge(y_kept, 2 * total + 1)
            nc.scalar.dma_start(sc.y[1][bass.ds(total * P, P), :], yo[:, :]).then_inc(y_stored, 16)
            act.wait_ge(y_stored, 32 * total + 16)
            close_wait(act, passed)

        @block.vector
        def _(dve):
            nc.vector.memset(h[:, :], 0.0).then_inc(h_zero, 1)
            dve.wait_ge(rows_loaded, 16)
            nc.vector.tensor_copy(slot_rows_f[:, :], slot_rows[:, :]).then_inc(rows_float, 1)
            dve.wait_ge(rows_turned, 1)
            nc.vector.tensor_copy(slots[:, :], p_x[:, 0:BLOCKS]).then_inc(slots_ready, 1)
            for q in range(PIECES):
                split_lo(dve, q, 0, 0)

            def keep_x(n):
                dve.wait_ge(xh_ready, n + 1)
                nc.vector.tensor_tensor(xtl[:, :, :], p_x[:, :].rearrange("p (c t) -> p c t", c=DC),
                                        xth[:, :, :].bitcast(F32), ALU.subtract).then_inc(xl_ready, 1)

            def keep_h(g):
                for i, (a, b) in enumerate(HT):
                    dve.wait_ge(hh_ready, 2 * g + i + 1)
                    nc.vector.tensor_tensor(htl[:, a:b, :],
                                            p_ht[i][:, 0:(b - a) * P].rearrange("p (m t) -> p m t", t=P),
                                            hth[:, a:b, :].bitcast(F32), ALU.subtract).then_inc(hl_ready, 1)

            def body(g, half, number, pieces):
                pieces = list(pieces)

                def some(n):
                    for q in pieces[:n]:
                        split_lo(dve, q, 1 - half, number + 1)
                    del pieces[:n]

                def mul(c):
                    dve.wait_ge(gate_ready, 2 * g + c + 1)
                    nc.vector.tensor_tensor(h[:, c * HN:(c + 1) * HN], p_up[c][1][:, 0:HN],
                                            gate[:, c * HN:(c + 1) * HN], ALU.mult).then_inc(h_ready, 1)

                some(1)
                keep_h(g)
                mul(0)
                some(2)
                mul(1)
                keep_x(g + 1)
                some(len(pieces))

            keep_x(0)
            passes(dve,
                   lambda g, row, half, number, ended: body(g, half, number, range(UP_PIECES)),
                   lambda g, row, half, number: body(g, half, number, range(UP_PIECES, PIECES)),
                   lambda g, row, half, number: body(g, half, number, ()))
            total = dve.value_load(bounds[0:1, EXPERTS:EXPERTS + 1], min_val=MIN_BLOCKS * EXPERTS, max_val=BLOCKS)
            keep_h(2 * total)


def rotary_tables():
    half = HD // 2
    f32 = np.float32
    inv_freq = f32(1.0) / (10000.0 ** (np.arange(half) / half)).astype(f32)
    freqs = np.outer(np.arange(SEQ, dtype=f32), inv_freq).astype(np.float64)
    freqs = np.concatenate([freqs, freqs], axis=-1)
    cos, sin = np.cos(freqs), np.sin(freqs)
    sin[:, :half] = -sin[:, :half]
    scale = ((np.arange(SEQ, dtype=f32) + f32(HD / 2)) / f32(HD))[:, None]
    scale = np.broadcast_to(scale, (SEQ, half))
    scale = np.stack([scale, f32(1.0) / scale], axis=-1).reshape(SEQ, HD).astype(f32)
    scale = scale.astype(np.float64)
    root = 1.0 / np.sqrt(HD)
    return np.stack([cos * scale * root, sin * scale * root, cos / scale, sin / scale]).astype(f32)


def stage_attention(nc, x, wq, wk, wv, wo, tables, out, sc):
    KVN = 2 * HD
    LAG = 2
    x_rows = x.rearrange("b s d -> (b s) d")
    out_rows = out.rearrange("b s d -> (b s) d")
    STEPS = SEQ_TILES
    KT = STEPS * (STEPS + 1) // 2
    tri = [i * (i + 1) // 2 for i in range(STEPS + 1)]
    with ExitStack() as ctx:
        def sb(name, shape, dt=F32):
            return ctx.enter_context(nc.sbuf_tensor(name, shape, dt))

        def sem(name):
            return ctx.enter_context(nc.semaphore(name))

        def bank(name, n=512):
            return ctx.enter_context(nc.psum_tensor(name, [P, n], F32))

        ident = sb("a_ident", [P, P])
        ident_r = sb("a_ident_r", [P, P], F32R)
        mask = sb("a_mask", [P, P])
        mask_r = sb("a_mask_r", [P, P], F32R)
        rot = sb("a_rot", [P, 4, STEPS, HD])
        xth = sb("a_xth", [P, DC, SEQ], F32R)
        xtl = sb("a_xtl", [P, DC, SEQ], F32R)
        raw = sb("a_raw", [P, DC, GROUP * HD + KVN])
        wqh = sb("a_wqh", [P, DC, GROUP * HD], F32R)
        wql = sb("a_wql", [P, DC, GROUP * HD], F32R)
        wkvh = sb("a_wkvh", [P, DC, KVN], F32R)
        wkvl = sb("a_wkvl", [P, DC, KVN], F32R)
        woh = sb("a_woh", [P, GROUP, DM], F32R)
        wol = sb("a_wol", [P, GROUP, DM], F32R)
        rc = sb("a_rc", [P, 5, HD])
        rs = sb("a_rs", [P, 5, HD])
        qk = sb("a_qk", [P, 5, HD])
        vr = sb("a_vr", [P, HD])
        qth = sb("a_qth", [P, GROUP, P], F32R)
        qtl = sb("a_qtl", [P, GROUP, P], F32R)
        kth = sb("a_kth", [P, SEQ], F32R)
        ktl = sb("a_ktl", [P, SEQ], F32R)
        vh = sb("a_vh", [P, STEPS, HD], F32R)
        vl = sb("a_vl", [P, STEPS, HD], F32R)
        prob = [sb(f"a_prob{n}", [P, GROUP, SEQ]) for n in range(2)]
        nmax = [sb(f"a_nmax{n}", [P, GROUP]) for n in range(2)]
        total = [sb(f"a_total{n}", [P, GROUP]) for n in range(2)]
        recip = [sb(f"a_recip{n}", [P, GROUP]) for n in range(2)]
        pth = [sb(f"a_pth{n}", [P, GROUP * P], F32R) for n in range(2)]
        ptl = [sb(f"a_ptl{n}", [P, GROUP * P], F32R) for n in range(2)]
        oth = [sb(f"a_oth{n}", [P, GROUP * P], F32R) for n in range(2)]
        otl = [sb(f"a_otl{n}", [P, GROUP * P], F32R) for n in range(2)]
        acc = sb("a_acc", [P, STEPS, DM])
        pos_in = sb("a_pos_in", [P, 2, TILES], I32)
        pos = sb("a_pos", [P, 2, TILES], I32)
        weight = sb("a_weight", [P, 2, TILES])
        idx = sb("a_idx", [P, 2], I32)
        wcol = sb("a_wcol", [P, 2])
        yg = [sb(f"a_yg{k}", [P, DM]) for k in range(2)]
        xo = sb("a_xo", [P, DM])

        p_s = [bank(f"a_ps{n}", 1024) for n in range(2)]
        p_pt = [bank(f"a_ppt{n}") for n in range(2)]
        p_o = bank("a_po")
        p_m = bank("a_pm")

        ident_done, ident_split, mask_done, mask_split = (
            sem("a_ident_done"), sem("a_ident_split"), sem("a_mask_done"), sem("a_mask_split"))
        tables_loaded, pos_ready, acc_zero = sem("a_tables_loaded"), sem("a_pos_ready"), sem("a_acc_zero")
        passed = sem("a_passed")
        x_loaded = [sem(f"a_x_loaded{i}") for i in range(STEPS)]
        qkv_loaded, qkv_hi, qkv_lo = sem("a_qkv_loaded"), sem("a_qkv_hi"), sem("a_qkv_lo")
        wo_loaded, wo_hi, wo_lo = sem("a_wo_loaded"), sem("a_wo_hi"), sem("a_wo_lo")
        projected, v_kept, roped, added = sem("a_projected"), sem("a_v_kept"), sem("a_roped"), sem("a_added")
        v_hi, v_split = sem("a_v_hi"), sem("a_v_split")
        qk_turned, qk_hi, qk_lo = sem("a_qk_turned"), sem("a_qk_hi"), sem("a_qk_lo")
        scored, maxed, exped = sem("a_scored"), sem("a_maxed"), sem("a_exped")
        inverted, normed = sem("a_inverted"), sem("a_normed")
        p_turned, p_hi, p_lo, p_used = sem("a_p_turned"), sem("a_p_hi"), sem("a_p_lo"), sem("a_p_used")
        o_hi, o_lo = sem("a_o_hi"), sem("a_o_lo")
        wo_done, acc_added = sem("a_wo_done"), sem("a_acc_added")
        idx_ready, gathered, summed = sem("a_idx_ready"), sem("a_gathered"), sem("a_summed")
        xo_loaded, mixed, silu_done, gated, out_ready, out_stored = (
            sem("a_xo_loaded"), sem("a_mixed"), sem("a_silu_done"), sem("a_gated"), sem("a_out_ready"),
            sem("a_out_stored"))

        block = ctx.enter_context(nc.Block())

        def heads(eng, plain, last):
            with eng.Fori(0, BATCH) as b:
                with eng.Fori(0, KV_HEADS - 1) as g:
                    plain(b * KV_HEADS + g)
                last(b * KV_HEADS + (KV_HEADS - 1))

        @block.sync
        def _(sp):
            def load_x(b, i):
                for dst, src in ((xth, sc.xt_hi), (xtl, sc.xt_lo)):
                    nc.sync.dma_start(dst[:, :, i * P:(i + 1) * P].bitcast(F32),
                                      src[:, bass.ds(b * SEQ + i * P, P)].rearrange("(c p) t -> p c t", p=P)
                                      ).then_inc(x_loaded[i], 16)

            def load_qkv(g):
                nc.sync.dma_start(raw[:, :, 0:GROUP * HD],
                                  wq[:, bass.ds(g * (GROUP * HD), GROUP * HD)].rearrange("(c p) n -> p c n", p=P)
                                  ).then_inc(qkv_loaded, 16)
                for n, w in enumerate((wk, wv)):
                    a = GROUP * HD + n * HD
                    nc.sync.dma_start(raw[:, :, a:a + HD], w[:, bass.ds(g * HD, HD)].rearrange("(c p) n -> p c n", p=P)
                                      ).then_inc(qkv_loaded, 16)

            def load_wo(g):
                nc.sync.dma_start(raw[:, :, 0:DM],
                                  wo[bass.ds(g * (GROUP * HD), GROUP * HD), :].rearrange("(h p) n -> p h n", p=P)
                                  ).then_inc(wo_loaded, 16)

            for f in range(4):
                nc.sync.dma_start(rot[:, f, :, :], tables[f, :, :].rearrange("(i p) d -> p i d", p=P)
                                  ).then_inc(tables_loaded, 16)
            load_x(0, 0)
            load_qkv(0)
            for i in range(1, STEPS):
                load_x(0, i)
            nc.sync.dma_start(pos_in[:, :, :].rearrange("p k t -> p (k t)"), sc.pos).then_inc(tables_loaded, 16)
            nc.sync.dma_start(weight[:, :, :].rearrange("p k t -> p (k t)"), sc.weight).then_inc(tables_loaded, 16)

            def plain(it):
                sp.wait_ge(qkv_lo, it + 1)
                load_wo(it % KV_HEADS)
                sp.wait_ge(wo_lo, it + 1)
                load_qkv((it + 1) % KV_HEADS)

            def last(it):
                b = it // KV_HEADS
                nxt = (b + 1) % BATCH
                plain(it)
                for i in range(STEPS):
                    sp.wait_ge(projected, 2 * STEPS * it + 2 * (i + 1))
                    load_x(nxt, i)
                    if i < LAG:
                        continue
                    load_xo(b, i - LAG)
                for j in range(STEPS - LAG, STEPS):
                    load_xo(b, j)

            def load_xo(b, j):
                c = b * STEPS + j
                sp.wait_ge(out_stored, 16 * c)
                nc.sync.dma_start(xo[:, :], x_rows[bass.ds(c * P, P), :]).then_inc(xo_loaded, 16)
                sp.wait_ge(out_ready, c + 1)
                nc.sync.dma_start(out_rows[bass.ds(c * P, P), :], xo[:, :]).then_inc(out_stored, 16)

            heads(sp, plain, last)
            sp.wait_ge(qkv_loaded, 48 * (BATCH * KV_HEADS + 1))
            for i in range(STEPS):
                sp.wait_ge(x_loaded[i], 32 * (BATCH + 1))
            sp.wait_ge(out_stored, 16 * TILES)

        @block.gpsimd
        def _(pool):
            make_identity(pool, ident, ident_done)
            nc.gpsimd.memset(mask[:, :], 0.0).then_inc(mask_done, 1)
            pool.wait_ge(mask_done, 1)
            nc.gpsimd.affine_select(out=mask[:, :], in_=mask[:, :], compare_op=ALU.is_ge, fill=NEG, base=0,
                                    pattern=[[-1, P]], channel_multiplier=1).then_inc(mask_done, 1)
            nc.gpsimd.memset(acc[:, :, :], 0.0).then_inc(acc_zero, 1)

            def norm(it, i, h):
                n = (i + 1) * P
                if h % 2 == 0:
                    pool.wait_ge(inverted, 2 * STEPS * it + 2 * i + h // 2 + 1)
                    close_wait(pool, passed)
                a = prob[i % 2][:, h, 0:n]
                nc.gpsimd.tensor_scalar(a, a, recip[i % 2][:, h:h + 1], 1.0, ALU.mult, ALU.mult).then_inc(normed, 1)

            def add(it, i):
                pool.wait_ge(qk_turned, 2 * STEPS * it + 2 * i)
                pool.wait_ge(roped, 2 * STEPS * it + 2 * i + 2)
                nc.gpsimd.tensor_tensor(qk[:, :, :], rc[:, :, :], rs[:, :, :], ALU.add).then_inc(added, 1)

            def split_v(it, i, used):
                pool.wait_ge(p_used, used)
                pool.wait_ge(v_kept, STEPS * it + i + 1)
                close_wait(pool, passed)
                nc.gpsimd.tensor_copy(vh[:, i, :], vr[:, :]).then_inc(v_hi, 1)
                pool.wait_ge(v_hi, STEPS * it + i + 1)
                nc.gpsimd.tensor_tensor(vl[:, i, :], vr[:, :], vh[:, i, :].bitcast(F32), ALU.subtract
                                        ).then_inc(v_split, 1)

            def gather(c):
                pool.wait_ge(out_ready, c)
                pool.wait_ge(pos_ready, 1)
                close_wait(pool, passed)
                nc.gpsimd.tensor_copy(idx[:, :], pos[:, :, bass.ds(c, 1)].rearrange("p k o -> p (k o)")).then_inc(idx_ready, 1)
                nc.gpsimd.tensor_copy(wcol[:, :], weight[:, :, bass.ds(c, 1)].rearrange("p k o -> p (k o)")).then_inc(idx_ready, 1)
                pool.wait_ge(idx_ready, 2 * c + 2)
                close_wait(pool, passed)
                for k in range(2):
                    nc.gpsimd.indirect_dma_start(yg[k][:, :], None, sc.y[0],
                                                 bass.IndirectOffsetOnAxis(idx[:, k:k + 1], 0)).then_inc(gathered, 16)

            def gather_more(c):
                pool.wait_ge(gathered, 32 * c + 32)
                close_wait(pool, passed)
                for k in range(2):
                    nc.gpsimd.indirect_dma_start(yg[k][:, :], None, sc.y[1],
                                                 bass.IndirectOffsetOnAxis(idx[:, k:k + 1], 0),
                                                 compute_op=ALU.add).then_inc(summed, 16)

            def step(it, i, combine):
                c = (it // KV_HEADS) * STEPS + i - LAG if combine and i >= LAG else None
                if c is not None:
                    gather(c)
                norm(it, i, 0)
                norm(it, i, 1)
                nit, ni = (it, i + 1) if i + 1 < STEPS else (it + 1, 0)
                add(nit, ni)
                if c is not None:
                    gather_more(c)
                norm(it, i, 2)
                norm(it, i, 3)
                split_v(nit, ni, KT * it + (0 if ni else KT))

            def finish(it):
                for j in range(STEPS - LAG, STEPS):
                    gather((it // KV_HEADS) * STEPS + j)
                    gather_more((it // KV_HEADS) * STEPS + j)

            add(0, 0)
            split_v(0, 0, 0)

            def plain(it):
                for i in range(STEPS):
                    step(it, i, False)

            def last(it):
                for i in range(STEPS):
                    step(it, i, True)
                finish(it)

            heads(pool, plain, last)
            pool.wait_ge(gathered, 32 * TILES)
            pool.wait_ge(summed, 32 * TILES)

        @block.tensor
        def _(pe):
            def project(it, i, m_free, o_free):
                if i == 0:
                    pe.wait_ge(qkv_lo, it + 1)
                pe.wait_ge(x_loaded[i], (it // KV_HEADS) * 32 + 32)
                pe.wait_ge(acc_added, m_free)
                t = slice(i * P, (i + 1) * P)
                for dst, n_out, ws, wl in ((p_m, GROUP * HD, wqh, wql), (p_o, KVN, wkvh, wkvl)):
                    if dst is p_o:
                        pe.wait_ge(o_lo, o_free)
                    n = 0
                    for d in range(DC):
                        for a, w in ((xth, ws), (xth, wl), (xtl, ws)):
                            last = nc.tensor.matmul(dst[:, 0:n_out], a[:, d, t], w[:, d, :],
                                                    start=(n == 0), stop=(n == 3 * DC - 1))
                            n += 1
                    last.then_inc(projected, 1)

            def turn_qk(it, i, p_count):
                pe.wait_ge(p_lo, p_count)
                pe.wait_ge(added, STEPS * it + i + 1)
                for h in range(GROUP):
                    last = nc.tensor.transpose(p_pt[0][:, h * P:(h + 1) * P], qk[:, h, :], ident[:, :])
                last.then_inc(qk_turned, 1)
                nc.tensor.transpose(p_pt[1][:, 0:P], qk[:, GROUP, :], ident[:, :]).then_inc(qk_turned, 1)

            def scores(it, i, h, begin=False):
                t4 = 4 * STEPS * it + 4 * i
                if h == 0:
                    pe.wait_ge(qk_lo, 2 * STEPS * it + 2 * i + 2)
                dst = p_s[h % 2]
                if not begin:
                    pe.wait_ge(exped, t4 + h - 1)
                width = (i + 1) * P
                for a in range(0, width, 512):
                    b = min(a + 512, width)
                    diagonal = b == width
                    parts = ((qth, kth), (qth, ktl), (qtl, kth))
                    for n, (q, k) in enumerate(parts):
                        last = nc.tensor.matmul(dst[:, a:b], q[:, h, :], k[:, a:b],
                                                start=(n == 0), stop=(n == 2 and not diagonal))
                    if diagonal:
                        last = nc.tensor.matmul(dst[:, b - P:b], ident_r[:, :], mask_r[:, :], start=False, stop=True)
                last.then_inc(scored, 1)

            def turn(it, i, k):
                s = (tri[i] + k) % 2
                if k >= 2:
                    pe.wait_ge(p_lo, KT * it + tri[i] + k - 1)
                for h in range(GROUP):
                    last = nc.tensor.transpose(p_pt[s][:, h * P:(h + 1) * P], prob[i % 2][:, h, k * P:(k + 1) * P],
                                               ident[:, :])
                last.then_inc(p_turned, 1)

            def turn_early(it, i, qk_count):
                pe.wait_ge(normed, 4 * STEPS * it + 4 * i + 4)
                pe.wait_ge(qk_lo, qk_count)
                for k in range(min(2, i + 1)):
                    turn(it, i, k)

            def values(it, i):
                n0 = KT * it + tri[i]

                def use(k):
                    s = (tri[i] + k) % 2
                    pe.wait_ge(p_lo, n0 + k + 1)
                    if k == 0:
                        pe.wait_ge(v_split, STEPS * it + i + 1)
                    for n, (v, p) in enumerate(((vh, pth), (vh, ptl), (vl, pth))):
                        last = nc.tensor.matmul(p_o[:, :], v[:, k, :], p[s][:, :],
                                                start=(k == 0 and n == 0), stop=(k == i and n == 2))
                    last.then_inc(p_used, 1)

                wait_kv()
                for k in range(i + 1):
                    use(k)
                    if k + 2 <= i:
                        turn(it, i, k + 2)

            wait_kv = None

            def wo_product(it, i):
                if i == 0:
                    pe.wait_ge(wo_lo, it + 1)
                pe.wait_ge(o_lo, STEPS * it + i + 1)
                pe.wait_ge(acc_added, STEPS * it + i)
                n = 0
                for h in range(GROUP):
                    for o, w in ((oth, woh), (oth, wol), (otl, woh)):
                        last = nc.tensor.matmul(p_m[:, :], o[i % 2][:, h * P:(h + 1) * P], w[:, h, :],
                                                start=(n == 0), stop=(n == 3 * GROUP - 1))
                        n += 1
                last.then_inc(wo_done, 1)

            def kv_read(n):
                def f():
                    pe.wait_ge(v_kept, n)
                    pe.wait_ge(roped, 2 * n)
                return f

            def body(it):
                nonlocal wait_kv
                t0 = STEPS * it
                for i in range(STEPS):
                    nit, ni = (it, i + 1) if i + 1 < STEPS else (it + 1, 0)
                    if i >= 1:
                        turn_early(it, i - 1, 2 * t0 + 2 * (i + 1))
                    project(nit, ni, t0 + max(0, i - 2), t0 + max(0, i - 1))
                    scores(it, i, 2)
                    scores(it, i, 3)
                    if i >= 1:
                        wait_kv = kv_read(t0 + i + 2)
                        values(it, i - 1)
                    turn_qk(nit, ni, KT * it + tri[i])
                    if i >= 2:
                        wo_product(it, i - 2)
                    scores(nit, ni, 0)
                    scores(nit, ni, 1)
                turn_early(it, STEPS - 1, 2 * t0 + 2 * (STEPS + 1))
                wo_product(it, STEPS - 2)
                wait_kv = kv_read(t0 + STEPS + 1)
                values(it, STEPS - 1)
                wo_product(it, STEPS - 1)

            pe.wait_ge(ident_done, 2)
            pe.wait_ge(ident_split, 1)
            pe.wait_ge(mask_split, 1)
            project(0, 0, 0, 0)
            turn_qk(0, 0, 0)
            scores(0, 0, 0, True)
            scores(0, 0, 1, True)
            heads(pe, body, body)

        @block.scalar
        def _(act):
            act.wait_ge(ident_done, 2)
            nc.scalar.activation(ident_r[:, :], ident[:, :], ACT.Copy).then_inc(ident_split, 1)
            act.wait_ge(mask_done, 2)
            nc.scalar.activation(mask_r[:, :], mask[:, :], ACT.Copy).then_inc(mask_split, 1)

            def keep_v(it, i):
                act.wait_ge(v_split, STEPS * it + i)
                act.wait_ge(projected, 2 * STEPS * it + 2 * i + 2)
                nc.scalar.activation(vr[:, :], p_o[:, HD:KVN], ACT.Copy).then_inc(v_kept, 1)

            def keep_qk(it, i):
                for n, (dst, width) in enumerate(((qth[:, :, :].rearrange("p h t -> p (h t)"), GROUP * P),
                                                  (kth[:, i * P:(i + 1) * P], P))):
                    act.wait_ge(qk_turned, 2 * STEPS * it + 2 * i + n + 1)
                    nc.scalar.activation(dst, p_pt[n][:, 0:width], ACT.Copy).then_inc(qk_hi, 1)

            def exp(it, i, h):
                n = (i + 1) * P
                act.wait_ge(maxed, 4 * STEPS * it + 4 * i + h + 1)
                nc.scalar.activation(prob[i % 2][:, h, 0:n], p_s[h % 2][:, 0:n], ACT.Exp,
                                     bias=nmax[i % 2][:, h:h + 1],
                                     accum_out=total[i % 2][:, h:h + 1]).then_inc(exped, 1)

            def keep_p(it, i, k):
                n = tri[i] + k
                if k >= 2 or i > 0:
                    act.wait_ge(p_used, KT * it + n - 1)
                act.wait_ge(p_turned, KT * it + n + 1)
                nc.scalar.activation(pth[n % 2][:, :], p_pt[n % 2][:, :], ACT.Copy).then_inc(p_hi, 1)

            def keep_o(it, i):
                act.wait_ge(wo_done, STEPS * it + max(0, i - 1))
                act.wait_ge(p_used, KT * it + tri[i + 1])
                nc.scalar.activation(oth[i % 2][:, :], p_o[:, :], ACT.Copy).then_inc(o_hi, 1)

            def split_qkv(it):
                act.wait_ge(projected, 2 * STEPS * it)
                act.wait_ge(qkv_loaded, 48 * it + 48)
                nc.scalar.activation(wqh[:, :, :], raw[:, :, 0:GROUP * HD], ACT.Copy).then_inc(qkv_hi, 1)
                nc.scalar.activation(wkvh[:, :, :], raw[:, :, GROUP * HD:GROUP * HD + KVN], ACT.Copy
                                     ).then_inc(qkv_hi, 1)

            def split_wo(it):
                act.wait_ge(wo_done, STEPS * it)
                act.wait_ge(wo_loaded, 16 * it + 16)
                nc.scalar.activation(woh[:, :, :], raw[:, :, 0:DM], ACT.Copy).then_inc(wo_hi, 1)

            def silu(c):
                act.wait_ge(mixed, 2 * c + 2)
                nc.scalar.activation(yg[0][:, :], yg[1][:, :], ACT.Silu).then_inc(silu_done, 1)

            def step(it, i, combine):
                nit, ni = (it, i + 1) if i + 1 < STEPS else (it + 1, 0)
                for k in range(min(2, i)):
                    keep_p(it, i - 1, k)
                keep_v(nit, ni)
                exp(it, i, 2)
                exp(it, i, 3)
                for k in range(2, i):
                    keep_p(it, i - 1, k)
                keep_qk(nit, ni)
                if i >= 1:
                    keep_o(it, i - 1)
                if i == STEPS - 2:
                    split_qkv(it + 1)
                if combine and i >= LAG:
                    silu((it // KV_HEADS) * STEPS + i - LAG)
                exp(nit, ni, 0)
                exp(nit, ni, 1)
                if i == 0:
                    split_wo(it)

            def body(it, combine):
                for i in range(STEPS):
                    step(it, i, combine)
                for k in range(STEPS):
                    keep_p(it, STEPS - 1, k)
                keep_o(it, STEPS - 1)
                if combine:
                    for j in range(STEPS - LAG, STEPS):
                        silu((it // KV_HEADS) * STEPS + j)

            split_qkv(0)
            keep_v(0, 0)
            keep_qk(0, 0)
            exp(0, 0, 0)
            exp(0, 0, 1)
            heads(act, lambda it: body(it, False), lambda it: body(it, True))

        @block.vector
        def _(dve):
            def rope(it, i):
                dve.wait_ge(added, STEPS * it + i)
                dve.wait_ge(projected, 2 * STEPS * it + 2 * i + 1)
                for first, count, src, table in ((0, GROUP, p_m, 0), (GROUP, 1, p_o, 2)):
                    if first:
                        dve.wait_ge(v_kept, STEPS * it + i + 1)
                    a = src[:, 0:count * HD].rearrange("p (h d) -> p h d", d=HD)
                    cos = rot[:, table, i, :].unsqueeze(1).to_broadcast([P, count, HD])
                    nc.vector.tensor_tensor(rc[:, first:first + count, :], a, cos, ALU.mult)
                    s = src[:, 0:count * HD].rearrange("p (h f d) -> p h f d", f=2, d=HD // 2)[:, :, ::-1, :]
                    sin = rot[:, table + 1, i, :].rearrange("p (f d) -> p f d", f=2).unsqueeze(1).to_broadcast(
                        [P, count, 2, HD // 2])
                    nc.vector.tensor_tensor(
                        rs[:, first:first + count, :].rearrange("p h (f d) -> p h f d", f=2), s, sin,
                        ALU.mult).then_inc(roped, 1)

            def maximum(it, i, h):
                dve.wait_ge(scored, 4 * STEPS * it + 4 * i + h + 1)
                nc.vector.tensor_reduce(nmax[i % 2][:, h:h + 1], p_s[h % 2][:, 0:(i + 1) * P], AX_X, ALU.max,
                                        negate=True).then_inc(maxed, 1)

            def invert(it, i, pair):
                dve.wait_ge(exped, 4 * STEPS * it + 4 * i + 2 * pair + 2)
                nc.vector.reciprocal(recip[i % 2][:, 2 * pair:2 * pair + 2],
                                     total[i % 2][:, 2 * pair:2 * pair + 2]).then_inc(inverted, 1)

            def keep_p(it, i, k):
                n = tri[i] + k
                dve.wait_ge(p_hi, KT * it + n + 1)
                nc.vector.tensor_tensor(ptl[n % 2][:, :], p_pt[n % 2][:, :], pth[n % 2][:, :].bitcast(F32),
                                        ALU.subtract).then_inc(p_lo, 1)

            def keep_qk(it, i):
                for n, (dst, hi, width) in enumerate((
                        (qtl[:, :, :].rearrange("p h t -> p (h t)"), qth[:, :, :].rearrange("p h t -> p (h t)"),
                         GROUP * P),
                        (ktl[:, i * P:(i + 1) * P], kth[:, i * P:(i + 1) * P], P))):
                    dve.wait_ge(qk_hi, 2 * STEPS * it + 2 * i + n + 1)
                    nc.vector.tensor_tensor(dst, p_pt[n][:, 0:width], hi.bitcast(F32), ALU.subtract).then_inc(qk_lo, 1)

            def keep_o(it, i):
                dve.wait_ge(o_hi, STEPS * it + i + 1)
                nc.vector.tensor_tensor(otl[i % 2][:, :], p_o[:, :], oth[i % 2][:, :].bitcast(F32), ALU.subtract
                                        ).then_inc(o_lo, 1)

            def accumulate(it, i):
                dve.wait_ge(wo_done, STEPS * it + i + 1)
                nc.vector.tensor_tensor(acc[:, i, :], acc[:, i, :], p_m[:, :], ALU.add).then_inc(acc_added, 1)

            def split_qkv(it):
                dve.wait_ge(qkv_hi, 2 * it + 2)
                nc.vector.tensor_tensor(wql[:, :, :], raw[:, :, 0:GROUP * HD], wqh[:, :, :].bitcast(F32), ALU.subtract)
                nc.vector.tensor_tensor(wkvl[:, :, :], raw[:, :, GROUP * HD:GROUP * HD + KVN],
                                        wkvh[:, :, :].bitcast(F32), ALU.subtract).then_inc(qkv_lo, 1)

            def split_wo(it):
                dve.wait_ge(wo_hi, it + 1)
                nc.vector.tensor_tensor(wol[:, :, :], raw[:, :, 0:DM], woh[:, :, :].bitcast(F32), ALU.subtract
                                        ).then_inc(wo_lo, 1)

            def mix(c):
                dve.wait_ge(summed, 32 * c + 32)
                nc.vector.tensor_scalar(yg[0][:, :], yg[0][:, :], wcol[:, 0:1], None, ALU.mult).then_inc(mixed, 1)
                dve.wait_ge(mixed, 2 * c + 1)
                nc.vector.scalar_tensor_tensor(out=yg[1][:, :], in0=yg[1][:, :], scalar=wcol[:, 1:2],
                                               in1=yg[0][:, :], op0=ALU.mult, op1=ALU.add).then_inc(mixed, 1)

            def gate(c, j, it):
                dve.wait_ge(silu_done, c + 1)
                dve.wait_ge(acc_added, STEPS * it + j + 1)
                nc.vector.tensor_tensor(yg[0][:, :], yg[0][:, :], acc[:, j, :], ALU.mult).then_inc(gated, 1)
                dve.wait_ge(xo_loaded, 16 * c + 16)
                dve.wait_ge(gated, 2 * c + 1)
                nc.vector.tensor_tensor(xo[:, :], xo[:, :], yg[0][:, :], ALU.add).then_inc(out_ready, 1)
                nc.vector.memset(acc[:, j, :], 0.0).then_inc(gated, 1)

            def step(it, i, combine):
                nit, ni = (it, i + 1) if i + 1 < STEPS else (it + 1, 0)
                invert(it, i, 0)
                for k in range(min(2, i)):
                    keep_p(it, i - 1, k)
                rope(nit, ni)
                maximum(it, i, 2)
                maximum(it, i, 3)
                for k in range(2, i):
                    keep_p(it, i - 1, k)
                invert(it, i, 1)
                keep_qk(nit, ni)
                if i >= 1:
                    keep_o(it, i - 1)
                if i >= 2:
                    accumulate(it, i - 2)
                if i == STEPS - 2:
                    split_qkv(it + 1)
                c = (it // KV_HEADS) * STEPS + i - LAG
                if combine and i >= LAG:
                    mix(c)
                maximum(nit, ni, 0)
                maximum(nit, ni, 1)
                if combine and i >= LAG:
                    gate(c, i - LAG, it)
                if i == 0:
                    split_wo(it)

            def body(it, combine):
                for i in range(STEPS):
                    step(it, i, combine)
                accumulate(it, STEPS - 2)
                for k in range(STEPS):
                    keep_p(it, STEPS - 1, k)
                keep_o(it, STEPS - 1)
                accumulate(it, STEPS - 1)
                if combine:
                    for j in range(STEPS - LAG, STEPS):
                        c = (it // KV_HEADS) * STEPS + j
                        mix(c)
                        gate(c, j, it)

            split_qkv(0)
            dve.wait_ge(tables_loaded, 96)
            nc.vector.tensor_scalar(pos[:, :, :], pos_in[:, :, :], float(P), None, ALU.add).then_inc(pos_ready, 1)
            dve.wait_ge(acc_zero, 1)
            rope(0, 0)
            keep_qk(0, 0)
            maximum(0, 0, 0)
            maximum(0, 0, 1)
            heads(dve, lambda it: body(it, False), lambda it: body(it, True))


def build(nc, x, wq, wk, wv, wo, gate_w, w1, w2, w3, tables, out):
    sc = Scratch(nc)
    stage_route(nc, x, gate_w, sc)
    stage_experts(nc, w1, w2, w3, sc)
    stage_attention(nc, x, wq, wk, wv, wo, tables, out, sc)


_INS = ["L0_attn_x", "L0_attn_Wq", "L0_attn_Wk", "L0_attn_Wv", "L0_attn_Wo", "L0_ffn_gate_w", "L0_ffn_w1",
        "L0_ffn_w2", "L0_ffn_w3"]
_OUTS = [((BATCH, SEQ, DM), "float32")]


def kernel(**inputs):
    import concourse.bacc as _bacc
    from concourse.bass_utils import run_bass_kernel_spmd as _run

    nc = _bacc.Bacc("TRN2", target_bir_lowering=False, num_devices=1)
    arrays, args = {}, []
    for name in _INS:
        a = np.ascontiguousarray(inputs[name])
        arrays[f"in_{name}"] = a
        args.append(nc.dram_tensor(f"in_{name}", a.shape, mybir.dt.from_np(a.dtype), kind="ExternalInput").ap())
    tables = rotary_tables()
    arrays["rotary_tables"] = tables
    args.append(nc.dram_tensor("rotary_tables", tables.shape, F32, kind="ExternalInput").ap())
    for i, (shape, dtype) in enumerate(_OUTS):
        args.append(nc.dram_tensor(f"out_{i}", shape, mybir.dt.from_np(np.dtype(dtype)), kind="ExternalOutput").ap())
    build(nc, *args)
    r = _run(nc, [arrays], core_ids=[0])
    return r.results[0]["out_0"]
```
